# Optimizing a Trainium2 kernel written in Bass

```python
import numpy as np
import jax
import jax.numpy as jnp

def _softmax(x, axis=-1):
    return jax.nn.softmax(x, axis=axis)

def _gelu(x):
    return jax.nn.gelu(x, approximate=True)

def _silu(x):
    return jax.nn.silu(x)

def _sigmoid(x):
    return jax.nn.sigmoid(x)

def _layernorm(x, axis=-1, eps=1e-05):
    m = jnp.mean(x, axis=axis, keepdims=True)
    v = jnp.var(x, axis=axis, keepdims=True)
    return (x - m) / jnp.sqrt(v + eps)

def _scatter_add(tgt, idx, src, axis=0):
    return tgt.at[idx].add(src)

def _segment_sum(src, seg, n):
    return jax.ops.segment_sum(src, seg, n)
kernel_name = 'mk_adaln_ffn_d1_seqx_r4_19da4c'

def setup_inputs(seed: int=0):
    np.random.seed(seed)
    _w = jnp.asarray

    def _rec_inputs():
        import jax
        import jax.numpy as jnp
        _rk = jax.random.key(seed)
        x = -7.109e-05 + 0.9999 * jax.random.normal(jax.random.fold_in(_rk, 1), (32, 64, 512), jnp.float32)
        _lenS = 64 - jax.random.randint(jax.random.fold_in(_rk, 7), (32,), 0, max(1, 64 // 4) + 1, jnp.int32)
        _lenS2 = 64 - jax.random.randint(jax.random.fold_in(_rk, 8), (32,), 0, max(1, 64 // 4) + 1, jnp.int32)
        itok_B_1_198 = jax.random.randint(jax.random.fold_in(_rk, 11), (32,), 1, 199, jnp.int32)
        return (x, itok_B_1_198)
    x, itok_B_1_198 = _rec_inputs()

    def _L0_cond_setup():
        import jax, jax.numpy as jnp
        import numpy as np
        B, C, T = (128, 64, 512)
        S, D = (200, 64)
        key = jax.random.key(seed)
        k1, k2, k3 = jax.random.split(key, 3)
        x = jax.random.normal(k1, (B, C, T), dtype=jnp.float32)
        conditions = jax.random.randint(k2, (B,), 0, S, dtype=jnp.int64)
        weights = jax.random.normal(k3, (S, C, D), dtype=jnp.float32) / jnp.sqrt(jnp.float32(C))
        return {'x': x, 'conditions': conditions, 'weights': weights}
    _L0_cond_all = _L0_cond_setup()
    _L0_cond_in = {k: v for k, v in _L0_cond_all.items() if k in ('weights',)}
    del _L0_cond_all

    def _L0_ffn_setup():
        import jax, jax.numpy as jnp
        import numpy as np
        HID = 512
        N_EXP = 32
        F_EXP = 192
        TOP_K = 6
        F_SH = 384
        B, S = (1, 256)
        key = jax.random.key(seed)
        ks = jax.random.split(key, 8)
        s = 0.02
        return {'hidden_states': jax.random.normal(ks[0], (B, S, HID), dtype=jnp.float32), 'gate_w': jax.random.normal(ks[1], (HID, N_EXP), dtype=jnp.float32) * s, 'wg': jax.random.normal(ks[2], (N_EXP, HID, F_EXP), dtype=jnp.float32) * s, 'wu': jax.random.normal(ks[3], (N_EXP, HID, F_EXP), dtype=jnp.float32) * s, 'wd': jax.random.normal(ks[4], (N_EXP, F_EXP, HID), dtype=jnp.float32) * s, 'sg': jax.random.normal(ks[5], (HID, F_SH), dtype=jnp.float32) * s, 'su': jax.random.normal(ks[6], (HID, F_SH), dtype=jnp.float32) * s, 'sd': jax.random.normal(ks[7], (F_SH, HID), dtype=jnp.float32) * s}
    _L0_ffn_all = _L0_ffn_setup()
    _L0_ffn_in = {k: v for k, v in _L0_ffn_all.items() if k in ('gate_w', 'wg', 'wu', 'wd', 'sg', 'su', 'sd')}
    del _L0_ffn_all
    return {'x': x, 'itok_B_1_198': itok_B_1_198, 'L0_cond_weights': _L0_cond_in['weights'], 'L0_ffn_gate_w': _L0_ffn_in['gate_w'], 'L0_ffn_wg': _L0_ffn_in['wg'], 'L0_ffn_wu': _L0_ffn_in['wu'], 'L0_ffn_wd': _L0_ffn_in['wd'], 'L0_ffn_sg': _L0_ffn_in['sg'], 'L0_ffn_su': _L0_ffn_in['su'], 'L0_ffn_sd': _L0_ffn_in['sd']}

def reference(x, itok_B_1_198, L0_cond_weights, L0_ffn_gate_w, L0_ffn_wg, L0_ffn_wu, L0_ffn_wd, L0_ffn_sg, L0_ffn_su, L0_ffn_sd):
    import jax
    import jax.numpy as jnp

    def _L0_cond_ref(x, conditions, weights):
        import jax, jax.numpy as jnp
        import numpy as np
        B, C, T = (128, 64, 512)
        S, D = (200, 64)
        w = weights[conditions]
        return jnp.einsum('bct,bcd->bdt', x, w)

    def _L0_ffn_ref(hidden_states, gate_w, wg, wu, wd, sg, su, sd):
        import jax, jax.numpy as jnp
        import numpy as np
        HID = 512
        N_EXP = 32
        F_EXP = 192
        TOP_K = 6
        F_SH = 384
        B, S = (1, 256)
        orig_shape = hidden_states.shape
        x = hidden_states.reshape(-1, HID)
        scores = jax.nn.sigmoid(x @ gate_w)
        topk_w, topk_i = jax.lax.top_k(scores, TOP_K)
        topk_w = topk_w / (jnp.sum(topk_w, axis=-1, keepdims=True) + 1e-20)
        combine = jnp.sum(jax.nn.one_hot(topk_i, N_EXP, dtype=topk_w.dtype) * topk_w[..., None], axis=1)
        g = jnp.einsum('td,edf->tef', x, wg)
        u = jnp.einsum('td,edf->tef', x, wu)
        act = jax.nn.silu(g) * u
        routed = jnp.einsum('tef,efd,te->td', act, wd, combine)
        routed = routed.reshape(orig_shape)
        shared = jax.nn.silu(hidden_states @ sg) * (hidden_states @ su) @ sd
        return routed + shared
    x = x + _L0_ffn_ref(_L0_cond_ref(x, itok_B_1_198, L0_cond_weights), L0_ffn_gate_w, L0_ffn_wg, L0_ffn_wu, L0_ffn_wd, L0_ffn_sg, L0_ffn_su, L0_ffn_sd)
    return x

_drawn_inputs = setup_inputs


def setup_inputs(seed=0):
    import zlib

    import numpy as np

    out = dict(_drawn_inputs(seed))
    spreads = {}
    factors = {'L0_ffn_gate_w': 5.004, 'L0_ffn_wg': 4.595, 'L0_ffn_wu': 4.495, 'L0_ffn_wd': 4.503}
    for name, (base, spread) in spreads.items():
        noise = np.random.default_rng([zlib.crc32(name.encode()), seed]).standard_normal(out[name].shape)
        drawn = base * np.exp(spread * noise) if base else spread * noise
        out[name] = jnp.asarray(drawn.astype(out[name].dtype))
    for name, factor in factors.items():
        out[name] = (out[name] * factor).astype(out[name].dtype)
    return out
```

```python
import concourse.bass as bass
from concourse import mybir
from contextlib import ExitStack


def adaln_moe_kernel(
    nc: bass.Bass,
    x: bass.AP,
    conditions: bass.AP,
    cond_weights: bass.AP,
    gate_w: bass.AP,
    wg: bass.AP,
    wu: bass.AP,
    wd: bass.AP,
    sg: bass.AP,
    su: bass.AP,
    sd: bass.AP,
    out: bass.AP,
):
    fp32 = mybir.dt.float32
    bf16 = mybir.dt.bfloat16
    i32 = mybir.dt.int32
    u32 = mybir.dt.uint32
    ALU = mybir.AluOpType
    ACT = mybir.ActivationFunctionType
    AX = mybir.AxisListType.X
    ds = bass.ds

    P = 128
    B, C, H = x.shape
    S = cond_weights.shape[0]
    E, _, F = wg.shape
    FS = sg.shape[1]
    T = B * C
    NT = T // P
    HC = H // P
    FC = 2
    FP = F // FC
    SC = FS // P
    TOPK = 6
    TILES = T * TOPK // P + E
    ROW = H + E
    GT = 4
    NG = NT // GT
    RING = 4
    UNROLL = 4
    AHEAD = 3
    AT_ONCE = 8
    EQUAL_ABOVE = 16.635532

    rows_d = nc.dram_tensor("rows", [T + P, ROW], fp32).ap()
    slots_d = nc.dram_tensor("slots", [P * TILES, 1], i32).ap()
    sums_d = [nc.dram_tensor(f"sum{n}", [T + P, H], fp32).ap() for n in range(2)]

    x_v = x.rearrange("(i b) c t -> (b c) i t", b=2)
    out_v = out.rearrange("(i b) c t -> (b c) i t", b=2)
    sums_v = [s[0:T, :].rearrange("(i p) t -> p i t", p=P) for s in sums_d]
    slots_v = slots_d.rearrange("(p j) o -> p (j o)", p=P)

    ctx = ExitStack()
    with ctx:
        def sb(name, shape, dt=fp32):
            return ctx.enter_context(nc.sbuf_tensor(name, shape, dt))

        def sem(name):
            return ctx.enter_context(nc.semaphore(name))

        x_all = sb("x_all", [P, NT, H])
        y_sb = sb("y_sb", [P, 4, H])
        yT = sb("yT", [P, HC, T])
        mix = sb("mix", [P, NT, P])
        cond_sb = sb("cond_sb", [1, B], i32)
        gate = sb("gate", [P, HC, E])
        wgu_sb = sb("wgu_sb", [P, RING, HC, 2 * F])
        wd_sb = sb("wd_sb", [FP, RING, FC, H])
        sgu_sb = sb("sgu_sb", [P, HC, 2 * FS])
        sd_sb = sb("sd_sb", [P, SC, H])
        hidT = sb("hidT", [P, 2, SC, GT * P])
        s_silu = sb("s_silu", [P, 2, GT * P])
        s_sum = sb("s_sum", [P, 2, H])
        zeros = sb("zeros", [P, ROW])
        logit = sb("logit", [P, NT, E])
        score = sb("score", [P, NT, E])
        best = sb("best", [P, NT, 8])
        best_i = sb("best_i", [P, NT, 8], u32)
        best_f = sb("best_f", [P, NT, 8])
        iota_e = sb("iota_e", [P, E])
        chosen = sb("chosen", [P, TOPK, NT, E], bf16)
        mask = sb("mask", [P, NT, E], bf16)
        msum = sb("msum", [P, 2, NT, E], bf16)
        wsum = sb("wsum", [P, NT])
        wrec = sb("wrec", [P, NT])
        combine = sb("combine", [P, NT, E])
        slot = sb("slot", [P, NT, E])
        picked = sb("picked", [P, NT, E])
        slot_k = sb("slot_k", [P, TOPK, NT])
        slot_i = sb("slot_i", [P, TOPK, NT], i32)
        slot_lo = sb("slot_lo", [P, TOPK, NT], i32)
        slot_hi = sb("slot_hi", [P, TOPK, NT], i32)
        before = sb("before", [P, P], bf16)
        ones = sb("ones", [P, P], bf16)
        ident = sb("ident", [P, P])
        steps = sb("steps", [E, T // P - 1])
        steps_lt = sb("steps_lt", [E, T // P - 1])
        count = sb("count", [E, 1])
        tiles_f = sb("tiles_f", [E, 1])
        tiles_b = sb("tiles_b", [E, P], bf16)
        first_col = sb("first_col", [E, 1])
        first_row = sb("first_row", [P, E])
        first_i = sb("first_i", [1, E], i32)
        iota_j = sb("iota_j", [E, P])
        reached = sb("reached", [E, P], bf16)
        tile_expert = sb("tile_expert", [P, P])
        tile_expert_i = sb("tile_expert_i", [1, P], i32)
        token_no = sb("token_no", [P, NT], i32)
        spare_no = sb("spare_no", [P, TILES], i32)
        slot_token = sb("slot_token", [P, TILES], i32)
        from_idx = [sb(f"from_idx{s}", [P, 1], i32) for s in range(UNROLL)]
        to_idx = [sb(f"to_idx{s}", [P, 1], i32) for s in range(UNROLL)]
        row = [sb(f"row{s}", [P, ROW]) for s in range(UNROLL)]
        hot = sb("hot", [P, E])
        weight = sb("weight", [P, 2])
        rowT = sb("rowT", [P, 2, HC, P])
        silu = sb("silu", [P, 2, F])
        act_sb = sb("act_sb", [P, 2, F])
        actT = sb("actT", [FP, 2, FC, P])
        result = [y_sb[:, s, :] for s in range(UNROLL)]

        bank = [ctx.enter_context(nc.psum_tensor(f"bank{i}", [P, 512], fp32)) for i in range(8)]
        Y_PS, YT_PS, LOGIT_PS = (bank[0], bank[1]), (bank[2], bank[3]), (bank[4], bank[5])
        RANK_PS, SMALL_PS, EXPERT_PS = bank[5], bank[6], bank[7]
        SG_PS, SU_PS, SD_PS = (bank[0], bank[1]), (bank[2], bank[3]), (bank[4], bank[7])
        XT_PS, GU_PS, AT_PS, D_PS = ((bank[2 * n], bank[2 * n + 1]) for n in range(4))

        x_in = [sem(f"x_in{n}") for n in range(4)]
        cond_in = sem("cond_in")
        mix_in = [sem(f"mix_in{n}") for n in range(2)]
        gate_in = sem("gate_in")
        shared_in = sem("shared_in")
        expert_in = [sem(f"expert_in{n}") for n in range(RING)]
        experts_loaded = sem("experts_loaded")
        mix_zero = sem("mix_zero")
        pool_c = sem("pool_c")
        consts = sem("consts")
        zeros_set = sem("zeros_set")
        y_done = sem("y_done")
        y_copied = sem("y_copied")
        yT_done = sem("yT_done")
        yT_copied = sem("yT_copied")
        logits_done = sem("logits_done")
        logits_copied = sem("logits_copied")
        y_stored = [sem(f"y_stored{n}") for n in range(4)]
        dve_c = sem("dve_c")
        clamped = sem("clamped")
        scored = sem("scored")
        mask_set = sem("mask_set")
        combine_set = sem("combine_set")
        rank_done = sem("rank_done")
        count_done = sem("count_done")
        tiles_set = sem("tiles_set")
        first_done = sem("first_done")
        reached_set = sem("reached_set")
        expert_done = sem("expert_done")
        tables_set = sem("tables_set")
        slots_set = sem("slots_set")
        inits_stored = sem("inits_stored")
        slots_init = sem("slots_init")
        combine_stored = sem("combine_stored")
        slots_stored = sem("slots_stored")
        slots_in = sem("slots_in")
        sg_done = sem("sg_done")
        su_done = sem("su_done")
        s_silu_set = sem("s_silu_set")
        hid_set = sem("hid_set")
        sd_done = sem("sd_done")
        s_sum_set = sem("s_sum_set")
        s_stored = [sem(f"s_stored{n}") for n in range(2)]
        from_idx_set = sem("from_idx_set")
        to_idx_set = sem("to_idx_set")
        slots_freed = sem("slots_freed")
        gathers_begun = sem("gathers_begun")
        adds_begun = sem("adds_begun")
        adds_ended = sem("adds_ended")
        row_in = [sem(f"row_in{s}") for s in range(UNROLL)]
        rowT_done = sem("rowT_done")
        rowT_set = sem("rowT_set")
        weight_set = sem("weight_set")
        gu_done = sem("gu_done")
        silu_set = sem("silu_set")
        act_set = sem("act_set")
        actT_done = sem("actT_done")
        actT_set = sem("actT_set")
        down_done = sem("down_done")
        result_set = sem("result_set")
        added = [sem(f"added{n}") for n in range(2)]
        sums_in = [sem(f"sums_in{n}") for n in range(NG)]
        total_set = sem("total_set")
        out_stored = sem("out_stored")

        block = ctx.enter_context(nc.Block())

        LAST = TILES // UNROLL - 1

        def over_tiles(engine, step):
            for s in range(UNROLL):
                step(0, s)
            with engine.Fori(1, LAST) as q:
                for s in range(UNROLL):
                    step(q, s)
            for s in range(UNROLL):
                step(LAST, s)

        def tile(q, s):
            q, s = q + s // UNROLL, s % UNROLL
            return q * UNROLL + s, q, s

        def first(j, n):
            return isinstance(j, int) and j < n

        def last_tile(j):
            return isinstance(j, int) and j == TILES - 1

        def adds_before(q, s):
            return q * 2 + s // 2

        def load_mix(engine, half):
            engine.wait_ge(mix_zero, 1)
            engine.wait_ge(cond_in, 16)
            with engine.Fori(0, B // 2 // AT_ONCE) as n:
                at = n * AT_ONCE + half * (B // 2)
                _, which = nc.values_load_multi_w_load_instructions(
                    cond_sb[0:1, ds(at, AT_ONCE)], engines=[engine.engine], min_val=0, max_val=S - 1)
                for k, c in enumerate(which):
                    i, h = n * (AT_ONCE // 2) + half * (NT // 2) + k // 2, k % 2
                    engine.dma_start(mix[h * C:(h + 1) * C, ds(i, 1), h * C:(h + 1) * C],
                                     cond_weights[ds(c, 1)].rearrange("s c d -> c s d")).then_inc(mix_in[half], 16)

        @block.sync
        def _(sp):
            sp.dma_start(cond_sb[:, :], conditions.rearrange("(o b) -> o b", o=1)).then_inc(cond_in, 16)
            for n in range(4):
                sp.dma_start(x_all[:, 4 * n:4 * n + 4, :], x_v[:, 4 * n:4 * n + 4, :]).then_inc(x_in[n], 16)
                if n == 0:
                    sp.dma_start(gate[:, :, :], gate_w.rearrange("(c p) e -> p c e", p=P)).then_inc(gate_in, 16)
            load_mix(sp, 1)
            for i in range(NT):
                sp.wait_ge(y_copied, i + 1)
                sp.dma_start(rows_d[i * P:(i + 1) * P, 0:H], y_sb[:, i % 4, :]).then_inc(y_stored[i % 4], 16)
                if i == 3:
                    sp.dma_start(sgu_sb[:, :, 0:FS], sg.rearrange("(c p) f -> p c f", p=P)).then_inc(shared_in, 16)
                    sp.dma_start(sgu_sb[:, :, FS:2 * FS], su.rearrange("(c p) f -> p c f", p=P)).then_inc(shared_in, 16)
                    sp.dma_start(sd_sb[:, :, :], sd.rearrange("(c p) h -> p c h", p=P)).then_inc(shared_in, 16)
                    sp.wait_ge(zeros_set, 1)
                    sp.dma_start(rows_d[T:T + P, :], zeros[:, :]).then_inc(inits_stored, 16)
                    sp.dma_start(sums_d[0][T:T + P, :], zeros[:, 0:H]).then_inc(inits_stored, 16)
                    sp.dma_start(sums_d[1][T:T + P, :], zeros[:, 0:H]).then_inc(inits_stored, 16)
                    sp.dma_start(sums_v[1], zeros[:, 0:H].rearrange("p (o h) -> p o h", o=1).to_broadcast([P, NT, H]))\
                        .then_inc(inits_stored, 16)

            def load_expert(e, s):
                sp.dma_start(wgu_sb[:, s, :, 0:F], wg[ds(e, 1)].rearrange("e (c p) f -> p (e c) f", p=P))\
                    .then_inc(expert_in[s], 16)
                sp.dma_start(wgu_sb[:, s, :, F:2 * F], wu[ds(e, 1)].rearrange("e (c p) f -> p (e c) f", p=P))\
                    .then_inc(expert_in[s], 16)
                sp.dma_start(wd_sb[:, s, :, :], wd[ds(e, 1)].rearrange("e (c p) h -> p (e c) h", p=FP))\
                    .then_inc(expert_in[s], 16)

            for e in range(RING):
                load_expert(e, e)
            sp.wait_ge(combine_set, 1)
            sp.dma_start(rows_d[0:T, H:ROW].rearrange("(i p) e -> p i e", p=P), combine[:, :, :])\
                .then_inc(combine_stored, 16)
            with sp.Fori(0, NT // 2) as q:
                for s in range(2):
                    sp.wait_ge(s_sum_set, q * 2 + s + 1)
                    sp.dma_start(sums_d[0][ds((q * 2 + s) * P, P), :], s_sum[:, s, :]).then_inc(s_stored[s], 16)
            for e in range(RING):
                sp.wait_ge(expert_in[e], 3 * 16)
                sp.sem_inc(experts_loaded, 1)
            sp.wait_ge(tables_set, 1)
            with sp.Fori(1, E // RING) as q:
                for s in range(RING):
                    tiles_before = sp.value_load(first_i[0:1, ds((q - 1) * RING + s + 1, 1)], min_val=1, max_val=TILES)
                    sp.wait_ge(down_done, tiles_before)
                    load_expert(q * RING + s, s)
                    sp.wait_ge(expert_in[s], (q + 1) * (3 * 16))
                    sp.sem_inc(experts_loaded, 1)
            for n in range(2):
                sp.wait_ge(added[n], 16 * (TILES // 2))
            for g in range(NG):
                for n, to in enumerate((x_all, yT.rearrange("p c (i h) -> p (c i) h", h=H))):
                    sp.dma_start(to[:, GT * g:GT * g + GT, :], sums_v[n][:, GT * g:GT * g + GT, :])\
                        .then_inc(sums_in[g], 16)
            for g in range(NG):
                sp.wait_ge(total_set, g + 1)
                sp.dma_start(out_v[:, GT * g:GT * g + GT, :], x_all[:, GT * g:GT * g + GT, :])\
                    .then_inc(out_stored, 16)
            sp.wait_ge(out_stored, 16 * NG)

        @block.gpsimd
        def _(pool):
            nc.gpsimd.memset(mix[:, :, :], 0.0).then_inc(mix_zero, 1)
            nc.gpsimd.memset(ident[:, :], 0.0).then_inc(pool_c, 1)
            nc.gpsimd.memset(zeros[:, :], 0.0).then_inc(zeros_set, 1)
            nc.gpsimd.memset(ones[:, :], 1.0).then_inc(pool_c, 1)
            pool.wait_ge(pool_c, 2)
            nc.gpsimd.affine_select(out=ident[:, :], in_=ident[:, :], compare_op=ALU.not_equal, fill=1.0,
                                    base=0, pattern=[[-1, P]], channel_multiplier=1).then_inc(consts, 1)
            nc.gpsimd.affine_select(out=before[:, :], in_=ones[:, :], compare_op=ALU.is_gt, fill=0.0,
                                    base=0, pattern=[[1, P]], channel_multiplier=-1).then_inc(consts, 1)
            nc.gpsimd.iota(iota_e[:, :], pattern=[[1, E]], base=0, channel_multiplier=0,
                           allow_small_or_imprecise_dtypes=True).then_inc(consts, 1)
            nc.gpsimd.iota(iota_j[:, :], pattern=[[1, P]], base=0, channel_multiplier=0,
                           allow_small_or_imprecise_dtypes=True).then_inc(consts, 1)
            nc.gpsimd.iota(steps[:, :], pattern=[[P, T // P - 1]], base=P, channel_multiplier=0,
                           allow_small_or_imprecise_dtypes=True).then_inc(consts, 1)
            nc.gpsimd.iota(token_no[:, :], pattern=[[P, NT]], base=0, channel_multiplier=1).then_inc(pool_c, 1)
            nc.gpsimd.iota(spare_no[:, :], pattern=[[0, TILES]], base=T, channel_multiplier=1).then_inc(pool_c, 1)
            pool.wait_ge(pool_c, 4)
            pool.dma_start(slots_v, spare_no[:, :]).then_inc(slots_init, 16)
            pool.wait_ge(slots_init, 16)
            pool.wait_ge(slots_set, 1)
            for k in range(TOPK):
                for i in range(NT):
                    pool.indirect_dma_start(
                        out=slots_d, out_offset=bass.IndirectOffsetOnAxis(ap=slot_i[:, k, i:i + 1], axis=0),
                        in_=token_no[:, i:i + 1], in_offset=None).then_inc(slots_stored, 16)
            pool.wait_ge(slots_stored, 16 * TOPK * NT)
            pool.dma_start(slot_token[:, :], slots_v).then_inc(slots_in, 16)
            pool.wait_ge(slots_in, 16)
            for n in range(4):
                pool.wait_ge(y_stored[n], 16 * NT // 4)
            pool.wait_ge(combine_stored, 16)
            pool.wait_ge(inits_stored, 16 * 4)

            def gather(q, s):
                j, q, s = tile(q, s)
                if not first(j, UNROLL):
                    pool.wait_ge(rowT_done, j - UNROLL + 1)
                    pool.wait_ge(weight_set, j - UNROLL + 1)
                    pool.sem_inc(slots_freed, 1)
                nc.gpsimd.tensor_copy(from_idx[s][:, :], slot_token[:, ds(j, 1)]).then_inc(from_idx_set, 1)
                pool.wait_ge(from_idx_set, j + 1)
                pool.sem_inc(gathers_begun, 1)
                pool.indirect_dma_start(
                    out=row[s][:, :], out_offset=None, in_=rows_d,
                    in_offset=bass.IndirectOffsetOnAxis(ap=from_idx[s][:, 0:1], axis=0)).then_inc(row_in[s], 16)

            def step(q, s):
                j = q * UNROLL + s
                if not (isinstance(j, int) and j + AHEAD >= TILES):
                    gather(q, s + AHEAD)
                if not first(j, 2):
                    pool.wait_ge(added[s % 2], adds_before(q, s) * 16)
                    pool.sem_inc(adds_ended, 1)
                nc.gpsimd.tensor_copy(to_idx[s][:, :], slot_token[:, ds(j, 1)]).then_inc(to_idx_set, 1)
                pool.wait_ge(to_idx_set, j + 1)
                pool.wait_ge(result_set, j + 1)
                pool.sem_inc(adds_begun, 1)
                pool.indirect_dma_start(
                    out=sums_d[s % 2], out_offset=bass.IndirectOffsetOnAxis(ap=to_idx[s][:, 0:1], axis=0),
                    in_=result[s], in_offset=None, compute_op=ALU.add).then_inc(added[s % 2], 16)

            for j in range(AHEAD):
                gather(0, j)
            for s in range(2):
                pool.wait_ge(s_stored[s], 16 * NT // 2)
            over_tiles(pool, step)

        @block.scalar
        def _(act):
            load_mix(act, 0)
            for i in range(NT):
                act.wait_ge(y_done, i + 1)
                if i >= 4:
                    act.wait_ge(y_stored[i % 4], 16 * (i // 4))
                    act.wait_ge(yT_done, i - 3)
                nc.scalar.copy(y_sb[:, i % 4, :], Y_PS[i % 2][:, :]).then_inc(y_copied, 1)
            act.wait_ge(clamped, NT)
            nc.scalar.activation(score[:, :, :], logit[:, :, :], ACT.Sigmoid).then_inc(scored, 1)
            for n in range(NG * SC):
                act.wait_ge(sg_done, n + 1)
                if n >= 2:
                    act.wait_ge(hid_set, n - 1)
                nc.scalar.activation(s_silu[:, n % 2, :], SG_PS[n % 2][:, :], ACT.Silu).then_inc(s_silu_set, 1)

            def store_result(q, s):
                j, q, s = tile(q, s)
                act.wait_ge(down_done, j + 1)
                if not first(j, UNROLL):
                    act.wait_ge(added[s % 2], (adds_before(q, s) - 1) * 16)
                nc.scalar.copy(result[s], D_PS[s % 2][:, :]).then_inc(result_set, 1)

            def step(q, s):
                j = q * UNROLL + s
                act.wait_ge(gu_done, j + 1)
                if not first(j, 2):
                    act.wait_ge(act_set, j - 1)
                nc.scalar.activation(silu[:, s % 2, :], GU_PS[s % 2][:, 0:F], ACT.Silu).then_inc(silu_set, 1)
                if not first(j, 1):
                    store_result(q, s - 1)

            over_tiles(act, step)
            store_result(LAST, UNROLL - 1)

        @block.vector
        def _(dve):
            chain = [0]

            def link(ins):
                chain[0] += 1
                ins.then_inc(dve_c, 1)
                dve.wait_ge(dve_c, chain[0])

            def rank_experts(i):
                dve.wait_ge(logits_done, i + 1)
                nc.vector.tensor_scalar(logit[:, i, :], LOGIT_PS[i % 2][:, 0:E], EQUAL_ABOVE, None, ALU.min)\
                    .then_inc(logits_copied, 1)
                dve.wait_ge(logits_copied, i + 1)
                link(nc.vector.max(best[:, i, :], logit[:, i, :]))
                nc.vector.max_index(best_i[:, i, :], best[:, i, :], logit[:, i, :]).then_inc(clamped, 1)

            for i in range(NT):
                dve.wait_ge(yT_done, i + 1)
                nc.vector.tensor_copy(yT[:, :, i * P:(i + 1) * P],
                                      YT_PS[i % 2].rearrange("p (c t) -> p c t", c=HC)).then_inc(yT_copied, 1)
                if i >= 2:
                    rank_experts(i - 2)
            rank_experts(NT - 2)
            rank_experts(NT - 1)

            dve.wait_ge(clamped, NT)
            link(nc.vector.tensor_copy(best_f[:, :, :], best_i[:, :, :]))
            dve.wait_ge(consts, 5)
            for k in range(TOPK):
                hot_k = nc.vector.tensor_tensor(
                    chosen[:, k, :, :], iota_e[:, :].rearrange("p (o e) -> p o e", o=1).to_broadcast([P, NT, E]),
                    best_f[:, :, k:k + 1].to_broadcast([P, NT, E]), ALU.is_equal)
            link(hot_k)
            at = chosen[:, 0, :, :]
            for k in range(1, TOPK):
                to = mask[:, :, :] if k == TOPK - 1 else msum[:, k % 2, :, :]
                adds = nc.vector.tensor_tensor(to, at, chosen[:, k, :, :], ALU.add)
                if k == TOPK - 1:
                    adds.then_inc(mask_set, 1)
                    dve.wait_ge(mask_set, 1)
                else:
                    link(adds)
                at = to
            dve.wait_ge(count_done, 1)
            link(nc.vector.tensor_copy(count[:, :], SMALL_PS[0:E, 0:1]))
            link(nc.vector.tensor_scalar(steps_lt[:, :], steps[:, :], count[:, 0:1], None, ALU.is_lt))
            link(nc.vector.tensor_reduce(count[:, :], steps_lt[:, :], AX, ALU.add))
            link(nc.vector.tensor_scalar(tiles_f[:, :], count[:, :], 1.0, None, ALU.add))
            nc.vector.tensor_copy(tiles_b[:, :], tiles_f[:, 0:1].to_broadcast([E, P])).then_inc(tiles_set, 1)
            dve.wait_ge(first_done, 1)
            link(nc.vector.tensor_copy(first_col[:, :], SMALL_PS[0:E, 1:2]))
            nc.vector.tensor_scalar(reached[:, :], iota_j[:, :], first_col[:, 0:1], None, ALU.is_ge)\
                .then_inc(reached_set, 1)
            link(nc.vector.tensor_copy(first_row[:, :], SMALL_PS[:, 32:32 + E]))
            nc.vector.tensor_copy(first_i[:, :], first_row[0:1, :])
            dve.wait_ge(rank_done, 1)
            link(nc.vector.scalar_tensor_tensor(
                slot[:, :, :], first_row[:, :].rearrange("p (o e) -> p o e", o=1).to_broadcast([P, NT, E]), float(P),
                RANK_PS.rearrange("p (i e) -> p i e", e=E), ALU.mult, ALU.add))
            for k in range(TOPK):
                link(nc.vector.tensor_tensor(picked[:, :, :], chosen[:, k, :, :], slot[:, :, :], ALU.mult))
                link(nc.vector.tensor_reduce(slot_k[:, k, :], picked[:, :, :], AX, ALU.add))
            link(nc.vector.tensor_copy(slot_i[:, :, :], slot_k[:, :, :]))
            nc.vector.tensor_scalar(slot_lo[:, :, :], slot_i[:, :, :], P - 1, TILES.bit_length() - 1,
                                    ALU.bitwise_and, ALU.logical_shift_left)
            link(nc.vector.tensor_scalar(slot_hi[:, :, :], slot_i[:, :, :], P.bit_length() - 1, None,
                                         ALU.logical_shift_right))
            nc.vector.tensor_tensor(slot_i[:, :, :], slot_lo[:, :, :], slot_hi[:, :, :], ALU.bitwise_or)\
                .then_inc(slots_set, 1)
            dve.wait_ge(expert_done, 1)
            link(nc.vector.tensor_scalar(tile_expert[:, :], EXPERT_PS[:, 0:P], -1.0, None, ALU.add))
            nc.vector.tensor_copy(tile_expert_i[:, :], tile_expert[0:1, :]).then_inc(tables_set, 1)
            dve.wait_ge(scored, 1)
            link(nc.vector.tensor_tensor(score[:, :, :], mask[:, :, :], score[:, :, :], ALU.mult))
            link(nc.vector.tensor_reduce(wsum[:, :], score[:, :, :], AX, ALU.add))
            link(nc.vector.tensor_scalar(wsum[:, :], wsum[:, :], 1e-20, None, ALU.add))
            link(nc.vector.reciprocal(wrec[:, :], wsum[:, :]))
            nc.vector.tensor_tensor(combine[:, :, :], score[:, :, :],
                                    wrec[:, :].rearrange("p (i o) -> p i o", o=1).to_broadcast([P, NT, E]),
                                    ALU.mult).then_inc(combine_set, 1)

            for g in range(NG):
                for f in range(SC):
                    n = g * SC + f
                    dve.wait_ge(s_silu_set, n + 1)
                    dve.wait_ge(su_done, n + 1)
                    if g >= 2:
                        dve.wait_ge(sd_done, GT * (g - 1))
                    nc.vector.tensor_tensor(hidT[:, g % 2, f, :], s_silu[:, n % 2, :], SU_PS[n % 2][:, :],
                                            ALU.mult).then_inc(hid_set, 1)
                for i in range(GT * g, GT * g + GT):
                    dve.wait_ge(sd_done, i + 1)
                    if i >= 2:
                        dve.wait_ge(s_stored[i % 2], 16 * (i // 2))
                    nc.vector.tensor_tensor(s_sum[:, i % 2, :], SD_PS[i % 2][:, :], x_all[:, i, :],
                                            ALU.add).then_inc(s_sum_set, 1)

            def weigh(q, s):
                j, q, s = tile(q, s)
                dve.wait_ge(row_in[s], (q + 1) * 16)
                if not first(j, 2):
                    dve.wait_ge(act_set, j - 1)
                    dve.wait_ge(weight_set, j)
                elif not first(j, 1):
                    dve.wait_ge(weight_set, j)
                nc.vector.scalar_tensor_tensor(
                    hot[:, :], iota_e[:, :], tile_expert[:, ds(j, 1)], row[s][:, H:ROW],
                    ALU.is_equal, ALU.mult, accum_out=weight[:, s % 2:s % 2 + 1]).then_inc(weight_set, 1)

            def copy_rowT(q, s):
                j, q, s = tile(q, s)
                dve.wait_ge(rowT_done, j + 1)
                if not first(j, 2):
                    dve.wait_ge(gu_done, j - 1)
                nc.vector.tensor_copy(rowT[:, s % 2, :, :], XT_PS[s % 2].rearrange("p (c t) -> p c t", c=HC))\
                    .then_inc(rowT_set, 1)

            def step(q, s):
                j = q * UNROLL + s
                if first(j, 1):
                    copy_rowT(q, s)
                    weigh(q, s)
                dve.wait_ge(silu_set, j + 1)
                dve.wait_ge(weight_set, j + 1)
                if not first(j, 2):
                    dve.wait_ge(actT_done, j - 1)
                nc.vector.scalar_tensor_tensor(
                    act_sb[:, s % 2, :], silu[:, s % 2, :], weight[:, s % 2:s % 2 + 1], GU_PS[s % 2][:, F:2 * F],
                    ALU.mult, ALU.mult).then_inc(act_set, 1)
                if not last_tile(j):
                    copy_rowT(q, s + 1)
                    weigh(q, s + 1)
                dve.wait_ge(actT_done, j + 1)
                if not first(j, 2):
                    dve.wait_ge(down_done, j - 1)
                nc.vector.tensor_copy(actT[:, s % 2, :, :],
                                      AT_PS[s % 2][0:FP, 0:FC * P].rearrange("p (c t) -> p c t", c=FC))\
                    .then_inc(actT_set, 1)

            over_tiles(dve, step)

            yflat = yT.rearrange("p c (i h) -> p (c i) h", h=H)
            for g in range(NG):
                dve.wait_ge(sums_in[g], 32)
                nc.vector.tensor_tensor(x_all[:, GT * g:GT * g + GT, :], x_all[:, GT * g:GT * g + GT, :],
                                        yflat[:, GT * g:GT * g + GT, :], ALU.add).then_inc(total_set, 1)

        @block.tensor
        def _(pe):
            def y_transposes(i):
                pe.wait_ge(y_copied, i + 1)
                if i >= 2:
                    pe.wait_ge(yT_copied, i - 1)
                for c in range(HC):
                    last = nc.tensor.transpose(YT_PS[i % 2][:, c * P:(c + 1) * P], y_sb[:, i % 4, c * P:(c + 1) * P],
                                               ident[:, :])
                last.then_inc(yT_done, 1)

            def logits(i):
                pe.wait_ge(yT_copied, i + 1)
                if i >= 2:
                    pe.wait_ge(logits_copied, i - 1)
                for c in range(HC):
                    last = nc.tensor.matmul(LOGIT_PS[i % 2][:, 0:E], yT[:, c, i * P:(i + 1) * P], gate[:, c, :],
                                            start=(c == 0), stop=(c == HC - 1))
                last.then_inc(logits_done, 1)

            pe.wait_ge(consts, 5)
            pe.wait_ge(gate_in, 16)
            for i in range(NT):
                if i % (NT // 2) == 0:
                    pe.wait_ge(mix_in[i // (NT // 2)], 16 * (B // 2))
                if i % 4 == 0:
                    pe.wait_ge(x_in[i // 4], 16)
                if i >= 2:
                    pe.wait_ge(y_copied, i - 1)
                nc.tensor.matmul(Y_PS[i % 2][:, :], mix[:, i, :], x_all[:, i, :], start=True, stop=True)\
                    .then_inc(y_done, 1)
                if i >= 1:
                    y_transposes(i - 1)
                if i >= 2:
                    logits(i - 2)
            y_transposes(NT - 1)
            logits(NT - 2)
            logits(NT - 1)

            pe.wait_ge(mask_set, 1)
            for i in range(NT):
                last = nc.tensor.matmul(SMALL_PS[0:E, 0:1], mask[:, i, :], ones[:, 0:1],
                                        start=(i == 0), stop=(i == NT - 1))
            last.then_inc(count_done, 1)
            nc.tensor.matmul(RANK_PS[:, :], before[:, :], mask[:, :, :].rearrange("p i e -> p (i e)"),
                             start=True, stop=False)
            for i in range(NT - 1):
                last = nc.tensor.matmul(RANK_PS[:, (i + 1) * E:NT * E], ones[:, :],
                                        mask[:, i:i + 1, :].to_broadcast([P, NT - 1 - i, E]),
                                        start=False, stop=(i == NT - 2))
            last.then_inc(rank_done, 1)
            pe.wait_ge(tiles_set, 1)
            nc.tensor.matmul(SMALL_PS[0:E, 1:2], before[0:E, 0:E], tiles_b[:, 0:1], start=True, stop=True)
            nc.tensor.matmul(SMALL_PS[:, 32:32 + E], tiles_b[:, :], before[0:E, 0:E], start=True, stop=True)\
                .then_inc(first_done, 1)
            pe.wait_ge(reached_set, 1)
            nc.tensor.matmul(EXPERT_PS[:, 0:P], ones[0:E, :], reached[:, :], start=True, stop=True)\
                .then_inc(expert_done, 1)

            pe.wait_ge(shared_in, 48)
            for g in range(NG):
                for f in range(SC):
                    n = g * SC + f
                    if n >= 2:
                        pe.wait_ge(hid_set, n - 1)
                    for ps, at, done in ((SG_PS, 0, sg_done), (SU_PS, FS, su_done)):
                        for c in range(HC):
                            last = nc.tensor.matmul(
                                ps[n % 2][:, :], sgu_sb[:, c, at + f * P:at + (f + 1) * P],
                                yT[:, c, g * GT * P:(g + 1) * GT * P], start=(c == 0), stop=(c == HC - 1))
                        last.then_inc(done, 1)
                pe.wait_ge(hid_set, SC * (g + 1))
                for i in range(GT * g, GT * g + GT):
                    if i >= 2:
                        pe.wait_ge(s_sum_set, i - 1)
                    t = i % GT
                    for f in range(SC):
                        last = nc.tensor.matmul(SD_PS[i % 2][:, :], hidT[:, g % 2, f, t * P:(t + 1) * P],
                                                sd_sb[:, f, :], start=(f == 0), stop=(f == SC - 1))
                    last.then_inc(sd_done, 1)

            pe.wait_ge(s_sum_set, NT)
            pe.wait_ge(tables_set, 1)

            def expert_of(j):
                return pe.value_load(tile_expert_i[0:1, ds(j, 1)], min_val=0, max_val=E - 1)

            def row_transposes(q, s):
                j, q, s = tile(q, s)
                pe.wait_ge(row_in[s], (q + 1) * 16)
                if not first(j, 2):
                    pe.wait_ge(rowT_set, j - 1)
                for c in range(HC):
                    last = nc.tensor.transpose(XT_PS[s % 2][:, c * P:(c + 1) * P], row[s][:, c * P:(c + 1) * P],
                                               ident[:, :])
                last.then_inc(rowT_done, 1)

            def gate_and_up(q, s, e):
                j, q, s = tile(q, s)
                pe.wait_ge(experts_loaded, e + 1)
                pe.wait_ge(rowT_set, j + 1)
                if not first(j, 2):
                    pe.wait_ge(act_set, j - 1)
                for c in range(HC):
                    last = nc.tensor.matmul(GU_PS[s % 2][:, 0:2 * F], rowT[:, s % 2, c, :],
                                            wgu_sb[:, ds(e % RING, 1), c, :].rearrange("p r f -> p (r f)"),
                                            start=(c == 0), stop=(c == HC - 1))
                last.then_inc(gu_done, 1)

            def down(q, s, e):
                j, q, s = tile(q, s)
                pe.wait_ge(actT_set, j + 1)
                if not first(j, 2):
                    pe.wait_ge(result_set, j - 1)
                for c in range(FC):
                    last = nc.tensor.matmul(D_PS[s % 2][:, :], actT[:, s % 2, c, :],
                                            wd_sb[:, ds(e % RING, 1), c, :].rearrange("p r h -> p (r h)"),
                                            start=(c == 0), stop=(c == FC - 1))
                last.then_inc(down_done, 1)

            def act_transposes(q, s):
                j, q, s = tile(q, s)
                pe.wait_ge(act_set, j + 1)
                if not first(j, 2):
                    pe.wait_ge(actT_set, j - 1)
                for c in range(FC):
                    last = nc.tensor.transpose(AT_PS[s % 2][0:FP, c * P:(c + 1) * P],
                                               act_sb[:, s % 2, c * FP:(c + 1) * FP], ident[:, :])
                last.then_inc(actT_done, 1)

            def step(q, s):
                j = q * UNROLL + s
                if first(j, 1):
                    row_transposes(q, s)
                gate_and_up(q, s, expert_of(j))
                if not last_tile(j):
                    row_transposes(q, s + 1)
                if not first(j, 1):
                    down(q, s - 1, expert_of(j - 1))
                act_transposes(q, s)

            over_tiles(pe, step)
            down(LAST, UNROLL - 1, expert_of(TILES - 1))


_INS = ['x', 'itok_B_1_198', 'L0_cond_weights', 'L0_ffn_gate_w', 'L0_ffn_wg', 'L0_ffn_wu', 'L0_ffn_wd',
        'L0_ffn_sg', 'L0_ffn_su', 'L0_ffn_sd']


def kernel(**inputs):
    import numpy as _np
    import concourse.bacc as _bacc
    from concourse import mybir as _mybir
    from concourse.bass_utils import run_bass_kernel_spmd as _run

    nc = _bacc.Bacc("TRN2", target_bir_lowering=False, num_devices=1)
    arrays, args = {}, []
    for name in _INS:
        a = _np.ascontiguousarray(inputs[name])
        arrays[f"in_{name}"] = a
        args.append(nc.dram_tensor(f"in_{name}", a.shape, _mybir.dt.from_np(a.dtype), kind="ExternalInput").ap())
    shape = inputs['x'].shape
    args.append(nc.dram_tensor("out_0", shape, _mybir.dt.float32, kind="ExternalOutput").ap())
    adaln_moe_kernel(nc, *args)
    r = _run(nc, [arrays], core_ids=[0])
    return r.results[0]["out_0"]
```

```python
import concourse.bass as bass
from concourse import mybir
from contextlib import ExitStack


def adaln_moe_kernel(
    nc: bass.Bass,
    x: bass.AP,
    conditions: bass.AP,
    cond_weights: bass.AP,
    gate_w: bass.AP,
    wg: bass.AP,
    wu: bass.AP,
    wd: bass.AP,
    sg: bass.AP,
    su: bass.AP,
    sd: bass.AP,
    out: bass.AP,
):
    fp32 = mybir.dt.float32
    fp32r = mybir.dt.float32r
    bf16 = mybir.dt.bfloat16
    i32 = mybir.dt.int32
    u32 = mybir.dt.uint32
    ALU = mybir.AluOpType
    ACT = mybir.ActivationFunctionType
    AX = mybir.AxisListType.X
    ds = bass.ds

    P = 128
    B, C, H = x.shape
    S = cond_weights.shape[0]
    E, _, F = wg.shape
    FS = sg.shape[1]
    T = B * C
    NT = T // P
    HC = H // P
    FC = 2
    FP = F // FC
    SC = FS // P
    TOPK = 6
    TILES = T * TOPK // P + E
    ROW = H + E
    GT = 4
    NG = NT // GT
    STEPS = NG * SC
    RING = 4
    SPLIT_AHEAD = 2
    WGU, WD = HC * 2 * F, FC * H
    UNROLL = 4
    LAST = TILES // UNROLL - 1
    LAG = 2
    HOTS = 4
    SETS = TOPK * NT // HOTS
    HOT_STEP = STEPS - TOPK
    EQUAL_ABOVE = 16.635532

    rows_d = nc.dram_tensor("rows", [T + P, ROW], fp32).ap()
    sums_d = [nc.dram_tensor(f"sum{n}", [T + P, H], fp32).ap() for n in range(2)]

    x_v = x.rearrange("(i b) c t -> (b c) i t", b=2)
    out_v = out.rearrange("(i b) c t -> (b c) i t", b=2)
    sums_v = [s[0:T, :].rearrange("(i p) t -> p i t", p=P) for s in sums_d]

    ctx = ExitStack()
    with ctx:
        def sb(name, shape, dt=fp32):
            return ctx.enter_context(nc.sbuf_tensor(name, shape, dt))

        def sem(name):
            return ctx.enter_context(nc.semaphore(name))

        SGU, SD, HID = HC * 2 * FS, SC * H, SC * GT * P
        arena = sb("arena", [P, 2 * (HC * T + SGU + SD + HID)], fp32r)

        def region(at, n):
            return arena[:, at:at + n]

        at = 0
        yT = [region(at + n * HC * T, HC * T).rearrange("p (c t) -> p c t", c=HC) for n in range(2)]
        at += 2 * HC * T
        sgu_at = at
        sgu = [region(at + n * SGU, SGU).rearrange("p (c f) -> p c f", c=HC) for n in range(2)]
        at += 2 * SGU
        sd_at = at
        sdw = [region(at + n * SD, SD).rearrange("p (c h) -> p c h", c=SC) for n in range(2)]
        at += 2 * SD
        hid = [region(at + n * HID, HID).rearrange("p (c t) -> p c t", c=SC) for n in range(2)]
        ring = region(0, RING * 2 * (WGU + WD)).rearrange("p (r s n) -> p r s n", r=RING, s=2)
        at = RING * 2 * (WGU + WD)
        rowT = [region(at + n * 2 * H, 2 * H).rearrange("p (b c t) -> p b c t", b=2, c=HC) for n in range(2)]
        at += 4 * H
        assert sgu_at < at <= sd_at
        at = sd_at
        actT = [arena[0:FP, at + n * 2 * FC * P:at + (n + 1) * 2 * FC * P]
                .rearrange("p (b c t) -> p b c t", b=2, c=FC) for n in range(2)]

        raw = sb("raw", [P, 2 * (WGU + WD)])
        raw_sgu = raw[:, 0:SGU].rearrange("p (c f) -> p c f", c=HC)
        raw_sd = raw[:, SGU:SGU + SD].rearrange("p (c h) -> p c h", c=SC)
        raw_ring = raw.rearrange("p (r n) -> p r n", r=2)

        x_sb = sb("x_sb", [P, 2, GT, H])
        y_sb = sb("y_sb", [P, 4, H])
        s_sum = y_sb[:, 0:2, :]
        result = [y_sb[:, s, :] for s in range(UNROLL)]
        yT_whole = sb("yT_whole", [P, 2, HC, P])
        mix = sb("mix", [P, NT, P])
        cond_sb = sb("cond_sb", [1, B], i32)
        gate = sb("gate", [P, HC, E])
        hid_f = sb("hid_f", [P, 2, GT * P])
        zeros = sb("zeros", [P, ROW])
        row = sb("row", [P, UNROLL, ROW])
        mix_flat = mix[:, :, :].rearrange("p i d -> p (i d)")
        hots_at = TOPK * NT * E // 2
        chosen = mix_flat[:, 0:hots_at].bitcast(bf16).rearrange("p (k i e) -> p k i e", k=TOPK, i=NT)
        msum = mix_flat[:, hots_at:hots_at + NT * E].bitcast(bf16).rearrange("p (b i e) -> p b i e", b=2, i=NT)
        logit, score, combine, slot = (row[:, n, 0:NT * E].rearrange("p (i e) -> p i e", i=NT) for n in range(4))
        best = sb("best", [P, NT, 8])
        best_i = sb("best_i", [P, NT, 8], u32)
        best_f = sb("best_f", [P, NT, 8])
        iota_e = sb("iota_e", [P, E])
        mask = sb("mask", [P, NT, E], bf16)
        wsum = sb("wsum", [P, NT])
        wrec = sb("wrec", [P, NT])
        picked = sb("picked", [P, NT, E])
        slot_k = sb("slot_k", [P, TOPK, NT])
        slot_i = sb("slot_i", [P, TOPK, NT], i32)
        slot_part_i = sb("slot_part_i", [P, 2, TOPK, NT], i32)
        slot_part = sb("slot_part", [P, 2, TOPK, NT])
        hots = sb("hots", [P, 2, HOTS, 2, P], fp32r)
        before = sb("before", [P, P], bf16)
        ones = sb("ones", [P, P], bf16)
        ident = sb("ident", [P, P])
        steps = sb("steps", [E, T // P - 1])
        steps_lt = sb("steps_lt", [E, T // P - 1])
        count = sb("count", [E, 1])
        tiles_f = sb("tiles_f", [E, 1])
        tiles_b = sb("tiles_b", [E, P], bf16)
        first_col = sb("first_col", [E, 1])
        first_row = sb("first_row", [P, E])
        iota_j = sb("iota_j", [P, P])
        token_no = sb("token_no", [P, NT])
        reached = sb("reached", [E, P], bf16)
        tile_expert = sb("tile_expert", [P, 1 + TILES])
        tile_expert_i = sb("tile_expert_i", [1, TILES], i32)
        to_split = sb("to_split", [1, 2, TILES])
        to_split_i = sb("to_split_i", [1, TILES], i32)
        found = sb("found", [P, TILES])
        spare = sb("spare", [P, TILES])
        slot_token = sb("slot_token", [P, TILES], i32)
        from_idx = [sb(f"from_idx{s}", [P, 1], i32) for s in range(UNROLL)]
        to_idx = [sb(f"to_idx{s}", [P, 1], i32) for s in range(UNROLL)]
        hot = sb("hot", [P, E])
        weight = sb("weight", [P, 2])
        act_sb = sb("act_sb", [P, 2, F])

        bank = [ctx.enter_context(nc.psum_tensor(f"bank{i}", [P, 512], fp32)) for i in range(8)]
        Y_PS, YT_PS, LOGIT_PS = (bank[0], bank[1]), (bank[2], bank[3]), (bank[4], bank[5])
        RANK_PS, SMALL_PS, EXPERT_PS, SLOT_PS = bank[5], bank[6], bank[6], bank[5]
        SG_PS, SU_PS, SD_PS = (bank[0], bank[1]), (bank[2], bank[3]), (bank[4], bank[7])
        XT_PS, GU_PS, AT_PS, D_PS = ((bank[2 * n], bank[2 * n + 1]) for n in range(4))

        cond_in = sem("cond_in")
        x_in = [sem(f"x_in{n}") for n in range(2)]
        mix_in = [sem(f"mix_in{n}") for n in range(NG)]
        gate_in = sem("gate_in")
        shared_in = sem("shared_in")
        expert_in = [sem(f"expert_in{n}") for n in range(2)]
        experts_loaded = sem("experts_loaded")
        mix_zero = sem("mix_zero")
        pool_c = sem("pool_c")
        consts = sem("consts")
        zeros_set = sem("zeros_set")
        y_done = sem("y_done")
        y_copied = sem("y_copied")
        yT_done = sem("yT_done")
        yT_whole_set = sem("yT_whole_set")
        yT_hi_set = sem("yT_hi_set")
        yT_lo_set = sem("yT_lo_set")
        shared_hi_set = sem("shared_hi_set")
        shared_lo_set = sem("shared_lo_set")
        logits_done = sem("logits_done")
        logits_copied = sem("logits_copied")
        y_stored = [sem(f"y_stored{n}") for n in range(4)]
        dve_c = sem("dve_c")
        ranked = sem("ranked")
        scored = sem("scored")
        mask_set = sem("mask_set")
        combine_set = sem("combine_set")
        rank_done = sem("rank_done")
        count_done = sem("count_done")
        tiles_set = sem("tiles_set")
        first_done = sem("first_done")
        first_copied = sem("first_copied")
        expert_done = sem("expert_done")
        tables_set = sem("tables_set")
        slot_part_set = sem("slot_part_set")
        place_hots_set = sem("place_hots_set")
        tile_hots_set = sem("tile_hots_set")
        found_done = sem("found_done")
        slots_set = sem("slots_set")
        inits_stored = sem("inits_stored")
        combine_stored = sem("combine_stored")
        sg_done = sem("sg_done")
        su_done = sem("su_done")
        s_silu_set = sem("s_silu_set")
        hid_set = sem("hid_set")
        hid_hi_set = sem("hid_hi_set")
        hid_lo_set = sem("hid_lo_set")
        sd_done = sem("sd_done")
        s_sum_set = sem("s_sum_set")
        s_stored = [sem(f"s_stored{n}") for n in range(2)]
        from_idx_set = sem("from_idx_set")
        to_idx_set = sem("to_idx_set")
        slots_freed = sem("slots_freed")
        gathers_begun = sem("gathers_begun")
        adds_begun = sem("adds_begun")
        adds_ended = sem("adds_ended")
        splits_begun = sem("splits_begun")
        gu_hi_set = sem("gu_hi_set")
        gu_lo_set = sem("gu_lo_set")
        d_hi_set = sem("d_hi_set")
        d_lo_set = sem("d_lo_set")
        row_in = [sem(f"row_in{s}") for s in range(UNROLL)]
        rowT_done = sem("rowT_done")
        rowT_hi_set = sem("rowT_hi_set")
        rowT_lo_set = sem("rowT_lo_set")
        weight_set = sem("weight_set")
        gu_done = sem("gu_done")
        silu_set = sem("silu_set")
        act_set = sem("act_set")
        actT_done = sem("actT_done")
        actT_hi_set = sem("actT_hi_set")
        actT_lo_set = sem("actT_lo_set")
        down_done = sem("down_done")
        result_set = sem("result_set")
        added = [sem(f"added{n}") for n in range(2)]
        sums_in = [sem(f"sums_in{n}") for n in range(2)]
        total_set = sem("total_set")
        out_stored = [sem(f"out_stored{n}") for n in range(2)]

        block = ctx.enter_context(nc.Block())

        def over_tiles(engine, step):
            for s in range(UNROLL):
                step(0, s)
            with engine.Fori(1, LAST) as q:
                for s in range(UNROLL):
                    step(q, s)
            for s in range(UNROLL):
                step(LAST, s)

        def tile(q, s):
            q, s = q + s // UNROLL, s % UNROLL
            return q * UNROLL + s, q, s

        def first(j, n):
            return isinstance(j, int) and j < n

        def exists(j):
            return not isinstance(j, int) or 0 <= j < TILES

        def adds_before(q, s):
            return q * 2 + s // 2

        def load_mix(engine, groups):
            engine.wait_ge(mix_zero, 1)
            engine.wait_ge(cond_in, 16)
            for g in groups:
                _, which = nc.values_load_multi_w_load_instructions(
                    cond_sb[0:1, g * 2 * GT:(g + 1) * 2 * GT], engines=[engine.engine], min_val=0, max_val=S - 1)
                for k, c in enumerate(which):
                    i, h = GT * g + k // 2, k % 2
                    engine.dma_start(mix[h * C:(h + 1) * C, i, h * C:(h + 1) * C],
                                     cond_weights[ds(c, 1)].rearrange("s c d -> (s c) d")).then_inc(mix_in[g], 16)

        SHARED_PIECES = [(n, min(512, SGU + SD - n)) for n in range(0, SGU + SD, 512)]
        SHARED_FROM = NT - 1 - len(SHARED_PIECES)

        def shared_piece(n, size):
            assert n + size <= SGU or n >= SGU
            if n < SGU:
                split = [region(sgu_at + part * SGU + n, size) for part in range(2)]
            else:
                split = [region(sd_at + part * SD + n - SGU, size) for part in range(2)]
            return raw[:, n:n + size], split[0], split[1]

        def gate_up_parts(e):
            return expert_parts(e, P, 0, WGU)

        def down_parts(e):
            return expert_parts(e, FP, WGU, WD)

        def expert_parts(e, p, n, size):
            return (raw_ring[0:p, ds(e % 2, 1), n:n + size].rearrange("p r n -> p (r n)"),
                    ring[0:p, ds(e % RING, 1), 0, n:n + size].rearrange("p r n -> p (r n)"),
                    ring[0:p, ds(e % RING, 1), 1, n:n + size].rearrange("p r n -> p (r n)"))

        @block.sync
        def _(sp):
            def load_x(g):
                sp.dma_start(x_sb[:, g % 2, :, :], x_v[:, GT * g:GT * g + GT, :]).then_inc(x_in[g % 2], 16)

            sp.dma_start(cond_sb[:, :], conditions.rearrange("(o b) -> o b", o=1)).then_inc(cond_in, 16)
            load_x(0)
            sp.dma_start(gate[:, :, :], gate_w.rearrange("(c p) e -> p c e", p=P)).then_inc(gate_in, 16)
            sp.wait_ge(mix_in[0], 16 * 2 * GT)
            load_x(1)
            sp.dma_start(raw_sgu[:, :, 0:FS], sg.rearrange("(c p) f -> p c f", p=P)).then_inc(shared_in, 16)
            sp.dma_start(raw_sgu[:, :, FS:2 * FS], su.rearrange("(c p) f -> p c f", p=P)).then_inc(shared_in, 16)
            sp.dma_start(raw_sd[:, :, :], sd.rearrange("(c p) h -> p c h", p=P)).then_inc(shared_in, 16)
            for i in range(NT):
                sp.wait_ge(y_copied, i + 1)
                sp.dma_start(rows_d[i * P:(i + 1) * P, 0:H], y_sb[:, i % 4, :]).then_inc(y_stored[i % 4], 16)
                if i % GT == GT - 1:
                    sp.wait_ge(y_done, i + 1)
                    load_x((i // GT + 2) % NG)
            sp.wait_ge(zeros_set, 1)
            sp.dma_start(rows_d[T:T + P, :], zeros[:, :]).then_inc(inits_stored, 16)
            sp.dma_start(sums_d[0][T:T + P, :], zeros[:, 0:H]).then_inc(inits_stored, 16)
            sp.dma_start(sums_d[1][T:T + P, :], zeros[:, 0:H]).then_inc(inits_stored, 16)
            sp.dma_start(sums_v[1], zeros[:, 0:H].rearrange("p (o h) -> p o h", o=1).to_broadcast([P, NT, H]))\
                .then_inc(inits_stored, 16)

            def load_expert(e, s):
                gu = raw_ring[:, s, 0:WGU].rearrange("p (c f) -> p c f", c=HC)
                down = raw_ring[0:FP, s, WGU:WGU + WD].rearrange("p (c h) -> p c h", c=FC)
                sp.dma_start(gu[:, :, 0:F], wg[ds(e, 1)].rearrange("e (c p) f -> p (e c) f", p=P))\
                    .then_inc(expert_in[s], 16)
                sp.dma_start(gu[:, :, F:2 * F], wu[ds(e, 1)].rearrange("e (c p) f -> p (e c) f", p=P))\
                    .then_inc(expert_in[s], 16)
                sp.dma_start(down, wd[ds(e, 1)].rearrange("e (c p) h -> p (e c) h", p=FP))\
                    .then_inc(expert_in[s], 16)

            sp.wait_ge(shared_lo_set, len(SHARED_PIECES))
            for e in range(2):
                load_expert(e, e)
            for e in range(2):
                sp.wait_ge(expert_in[e], 3 * 16)
                sp.sem_inc(experts_loaded, 1)
            for g in range(NG):
                for i in range(GT * g, GT * g + GT):
                    sp.wait_ge(s_sum_set, i + 1)
                    sp.dma_start(sums_d[0][i * P:(i + 1) * P, :], s_sum[:, i % 2, :]).then_inc(s_stored[i % 2], 16)
                if g < NG - 2:
                    load_x(g + 2)
                if g == 1:
                    sp.wait_ge(combine_set, 1)
                    sp.dma_start(rows_d[0:T, H:ROW].rearrange("(i p) e -> p i e", p=P), combine)\
                        .then_inc(combine_stored, 16)
            with sp.Fori(1, E // 2) as q:
                for s in range(2):
                    sp.wait_ge(gu_lo_set, q * 2 + s - 1)
                    sp.wait_ge(d_lo_set, q * 2 + s - 1)
                    load_expert(q * 2 + s, s)
                    sp.wait_ge(expert_in[s], (q + 1) * (3 * 16))
                    sp.sem_inc(experts_loaded, 1)
            for n in range(2):
                sp.wait_ge(added[n], 16 * (TILES // 2))
            sp.wait_ge(d_lo_set, E)

            def load_sums(g):
                if g >= 2:
                    sp.wait_ge(out_stored[g % 2], 16 * (g // 2))
                second = raw_ring[:, g % 2, 0:GT * H].rearrange("p (i h) -> p i h", h=H)
                sp.dma_start(x_sb[:, g % 2, :, :], sums_v[0][:, GT * g:GT * g + GT, :]).then_inc(sums_in[g % 2], 16)
                sp.dma_start(second, sums_v[1][:, GT * g:GT * g + GT, :]).then_inc(sums_in[g % 2], 16)

            load_sums(0)
            load_sums(1)
            for g in range(NG):
                sp.wait_ge(total_set, g + 1)
                sp.dma_start(out_v[:, GT * g:GT * g + GT, :], x_sb[:, g % 2, :, :]).then_inc(out_stored[g % 2], 16)
                if g + 2 < NG:
                    load_sums(g + 2)
            for n in range(2):
                sp.wait_ge(out_stored[n], 16 * NG // 2)

        @block.gpsimd
        def _(pool):
            nc.gpsimd.memset(mix[:, :, :], 0.0).then_inc(mix_zero, 1)
            nc.gpsimd.memset(ident[:, :], 0.0).then_inc(pool_c, 1)
            nc.gpsimd.memset(ones[:, :], 1.0).then_inc(pool_c, 1)
            pool.wait_ge(pool_c, 2)
            nc.gpsimd.affine_select(out=ident[:, :], in_=ident[:, :], compare_op=ALU.not_equal, fill=1.0,
                                    base=0, pattern=[[-1, P]], channel_multiplier=1).then_inc(consts, 1)
            load_mix(pool, range(1, NG, 2))
            nc.gpsimd.affine_select(out=before[:, :], in_=ones[:, :], compare_op=ALU.is_gt, fill=0.0,
                                    base=0, pattern=[[1, P]], channel_multiplier=-1).then_inc(consts, 1)
            nc.gpsimd.memset(zeros[:, :], 0.0).then_inc(zeros_set, 1)
            for to, pattern, base, down in (
                    (iota_e, [[1, E]], 0, 0), (iota_j, [[1, P]], 0, 0), 
                    (token_no, [[P, NT]], 1, 1), (steps, [[P, T // P - 1]], P, 0),
                    (spare, [[0, TILES]], T + 1, 1)):
                nc.gpsimd.iota(to[:, :], pattern=pattern, base=base, channel_multiplier=down,
                               allow_small_or_imprecise_dtypes=True).then_inc(consts, 1)
            for n, size in SHARED_PIECES:
                whole, hi, lo = shared_piece(n, size)
                pool.wait_ge(shared_hi_set, n // 512 + 1)
                nc.gpsimd.tensor_tensor(lo, whole, hi.bitcast(fp32), ALU.subtract).then_inc(shared_lo_set, 1)
            pool.wait_ge(slot_part_set, 1)
            for n in range(SETS):
                k, part = n // (NT // HOTS), n % (NT // HOTS)
                if n >= 2:
                    pool.wait_ge(found_done, n - 1)
                for h in range(HOTS):
                    i = part * HOTS + h
                    last = nc.gpsimd.tensor_scalar(hots[:, n % 2, h, 0, :], iota_j[:, :], slot_part[:, 0, k, i:i + 1],
                                                   None, ALU.is_equal)
                last.then_inc(place_hots_set, 1)
            pool.wait_ge(slots_set, 1)
            for n in range(4):
                pool.wait_ge(y_stored[n], 16 * NT // 4)
            pool.wait_ge(combine_stored, 16)
            pool.wait_ge(inits_stored, 16 * 4)

            def gather(q, s):
                j, q, s = tile(q, s)
                if not first(j, UNROLL):
                    pool.wait_ge(rowT_done, j - UNROLL + 1)
                    pool.wait_ge(weight_set, j - UNROLL + 1)
                    pool.sem_inc(slots_freed, 1)
                nc.gpsimd.tensor_copy(from_idx[s][:, :], slot_token[:, ds(j, 1)]).then_inc(from_idx_set, 1)
                pool.wait_ge(from_idx_set, j + 1)
                pool.sem_inc(gathers_begun, 1)
                pool.indirect_dma_start(
                    out=row[:, s, :], out_offset=None, in_=rows_d,
                    in_offset=bass.IndirectOffsetOnAxis(ap=from_idx[s][:, 0:1], axis=0)).then_inc(row_in[s], 16)

            def scatter(q, s):
                j, q, s = tile(q, s)
                if not first(j, 2):
                    pool.wait_ge(added[s % 2], adds_before(q, s) * 16)
                    pool.sem_inc(adds_ended, 1)
                nc.gpsimd.tensor_copy(to_idx[s][:, :], slot_token[:, ds(j, 1)]).then_inc(to_idx_set, 1)
                pool.wait_ge(to_idx_set, j + 1)
                pool.wait_ge(result_set, j + 1)
                pool.sem_inc(adds_begun, 1)
                pool.indirect_dma_start(
                    out=sums_d[s % 2], out_offset=bass.IndirectOffsetOnAxis(ap=to_idx[s][:, 0:1], axis=0),
                    in_=result[s], in_offset=None, compute_op=ALU.add).then_inc(added[s % 2], 16)

            def step(q, s):
                j = q * UNROLL + s
                if exists(j + UNROLL):
                    gather(q, s + UNROLL)
                if not first(j, LAG):
                    scatter(q, s - LAG)

            for j in range(UNROLL):
                gather(0, j)
            for s in range(2):
                pool.wait_ge(s_stored[s], 16 * NT // 2)
            over_tiles(pool, step)
            for s in range(UNROLL - LAG, UNROLL):
                scatter(LAST, s)

        @block.scalar
        def _(act):
            load_mix(act, range(0, NG, 2))

            def yT_high(i):
                act.wait_ge(yT_whole_set, i + 1)
                nc.scalar.copy(yT[0][:, :, i * P:(i + 1) * P], yT_whole[:, i % 2, :, :])\
                    .then_inc(yT_hi_set, 1)

            for i in range(NT):
                act.wait_ge(y_done, i + 1)
                if i >= 4:
                    act.wait_ge(y_stored[i % 4], 16 * (i // 4))
                    act.wait_ge(yT_done, i - 3)
                nc.scalar.copy(y_sb[:, i % 4, :], Y_PS[i % 2][:, :]).then_inc(y_copied, 1)
                if i >= 1:
                    yT_high(i - 1)
                if SHARED_FROM <= i < SHARED_FROM + len(SHARED_PIECES):
                    act.wait_ge(shared_in, 48)
                    whole, hi, _ = shared_piece(*SHARED_PIECES[i - SHARED_FROM])
                    nc.scalar.copy(hi, whole).then_inc(shared_hi_set, 1)
            yT_high(NT - 1)
            act.wait_ge(ranked, NT)
            nc.scalar.activation(score, logit, ACT.Sigmoid).then_inc(scored, 1)
            for n in range(STEPS):
                g, f = n // SC, n % SC
                act.wait_ge(sg_done, n + 1)
                if n >= 2:
                    act.wait_ge(hid_lo_set, n - 1)
                nc.scalar.activation(hid_f[:, n % 2, :], SG_PS[n % 2][:, :], ACT.Silu).then_inc(s_silu_set, 1)
                act.wait_ge(hid_set, n + 1)
                if g >= 1:
                    act.wait_ge(sd_done, GT * g)
                nc.scalar.copy(hid[0][:, f, :], hid_f[:, n % 2, :]).then_inc(hid_hi_set, 1)

            def gate_up_high(e):
                whole, hi, _ = gate_up_parts(e)
                nc.scalar.copy(hi, whole).then_inc(gu_hi_set, 1)

            def down_high(e):
                whole, hi, _ = down_parts(e)
                nc.scalar.copy(hi, whole).then_inc(d_hi_set, 1)

            act.wait_ge(su_done, STEPS)
            for e in range(SPLIT_AHEAD):
                act.wait_ge(experts_loaded, e + 1)
                gate_up_high(e)
                down_high(e)
            act.wait_ge(tables_set, 1)
            for s in range(2):
                act.wait_ge(s_stored[s], 16 * NT // 2)

            def rowT_high(q, s):
                j, q, s = tile(q, s)
                act.wait_ge(rowT_done, j + 1)
                if not first(j, 2):
                    act.wait_ge(gu_done, j - 1)
                nc.scalar.copy(rowT[0][:, s % 2, :, :], XT_PS[s % 2].rearrange("p (c t) -> p c t", c=HC))\
                    .then_inc(rowT_hi_set, 1)

            def store_result(q, s):
                j, q, s = tile(q, s)
                act.wait_ge(down_done, j + 1)
                if not first(j, UNROLL):
                    act.wait_ge(added[s % 2], (adds_before(q, s) - 1) * 16)
                nc.scalar.copy(result[s], D_PS[s % 2][:, :]).then_inc(result_set, 1)

            def actT_high(q, s):
                j, q, s = tile(q, s)
                act.wait_ge(actT_done, j + 1)
                if not first(j, 2):
                    act.wait_ge(down_done, j - 1)
                nc.scalar.copy(actT[0][:, s % 2, :, :],
                               AT_PS[s % 2][0:FP, 0:FC * P].rearrange("p (c t) -> p c t", c=FC))\
                    .then_inc(actT_hi_set, 1)

            def step(q, s):
                j = q * UNROLL + s
                if first(j, 1):
                    rowT_high(0, 0)
                    rowT_high(0, 1)
                act.wait_ge(gu_done, j + 1)
                if not first(j, 2):
                    act.wait_ge(actT_done, j - 1)
                nc.scalar.activation(act_sb[:, s % 2, :], GU_PS[s % 2][:, 0:F], ACT.Silu).then_inc(silu_set, 1)
                if not first(j, 1):
                    actT_high(q, s - 1)
                if exists(j + 2):
                    rowT_high(q, s + 2)
                e = act.value_load(to_split_i[0:1, ds(j, 1)], min_val=0, max_val=E - 1)
                with act.If(e > 0):
                    act.wait_ge(experts_loaded, e + 1)
                    act.wait_ge(gu_done, j + 1)
                    act.sem_inc(splits_begun, 1)
                    gate_up_high(e)
                if not first(j, 2):
                    store_result(q, s - 2)
                with act.If(e > 0):
                    if not first(j, 2):
                        act.wait_ge(down_done, j - 1)
                        act.sem_inc(splits_begun, 1)
                    down_high(e)

            over_tiles(act, step)
            actT_high(LAST, UNROLL - 1)
            store_result(LAST, UNROLL - 2)
            store_result(LAST, UNROLL - 1)

        @block.vector
        def _(dve):
            chain = [0]

            def link(ins):
                chain[0] += 1
                ins.then_inc(dve_c, 1)
                dve.wait_ge(dve_c, chain[0])

            def subtract(lo, whole, hi):
                return nc.vector.tensor_tensor(lo, whole, hi.bitcast(fp32), ALU.subtract)

            def transposed(i):
                dve.wait_ge(yT_done, i + 1)
                if i >= 2:
                    dve.wait_ge(logits_done, i - 1)
                nc.vector.tensor_copy(yT_whole[:, i % 2, :, :], YT_PS[i % 2].rearrange("p (c t) -> p c t", c=HC))\
                    .then_inc(yT_whole_set, 1)

            def yT_low(i):
                dve.wait_ge(yT_hi_set, i + 1)
                subtract(yT[1][:, :, i * P:(i + 1) * P], yT_whole[:, i % 2, :, :], yT[0][:, :, i * P:(i + 1) * P])\
                    .then_inc(yT_lo_set, 1)

            def rank_experts(i):
                dve.wait_ge(logits_done, i + 1)
                nc.vector.tensor_scalar(logit[:, i, :], LOGIT_PS[i % 2][:, 0:E], EQUAL_ABOVE, None, ALU.min)\
                    .then_inc(logits_copied, 1)
                dve.wait_ge(logits_copied, i + 1)
                link(nc.vector.max(best[:, i, :], logit[:, i, :]))
                nc.vector.max_index(best_i[:, i, :], best[:, i, :], logit[:, i, :]).then_inc(ranked, 1)

            for i in range(NT):
                transposed(i)
                if i >= 1:
                    yT_low(i - 1)
                    rank_experts(i - 1)
            yT_low(NT - 1)
            rank_experts(NT - 1)

            dve.wait_ge(ranked, NT)
            link(nc.vector.tensor_copy(best_f[:, :, :], best_i[:, :, :]))
            dve.wait_ge(consts, 7)
            for k in range(TOPK):
                hot_k = nc.vector.tensor_tensor(
                    chosen[:, k, :, :], iota_e[:, :].rearrange("p (o e) -> p o e", o=1).to_broadcast([P, NT, E]),
                    best_f[:, :, k:k + 1].to_broadcast([P, NT, E]), ALU.is_equal)
            link(hot_k)
            at = chosen[:, 0, :, :]
            for k in range(1, TOPK):
                to = mask[:, :, :] if k == TOPK - 1 else msum[:, k % 2, :, :]
                adds = nc.vector.tensor_tensor(to, at, chosen[:, k, :, :], ALU.add)
                if k == TOPK - 1:
                    adds.then_inc(mask_set, 1)
                else:
                    link(adds)
                at = to

            def count_tiles():
                dve.wait_ge(count_done, 1)
                link(nc.vector.tensor_copy(count[:, :], SMALL_PS[0:E, 0:1]))
                link(nc.vector.tensor_scalar(steps_lt[:, :], steps[:, :], count[:, 0:1], None, ALU.is_lt))
                link(nc.vector.tensor_reduce(count[:, :], steps_lt[:, :], AX, ALU.add))
                link(nc.vector.tensor_scalar(tiles_f[:, :], count[:, :], 1.0, None, ALU.add))
                nc.vector.tensor_copy(tiles_b[:, :], tiles_f[:, 0:1].to_broadcast([E, P])).then_inc(tiles_set, 1)

            def first_tiles():
                dve.wait_ge(first_done, 1)
                link(nc.vector.tensor_copy(first_col[:, :], SMALL_PS[0:E, 1:2]))
                link(nc.vector.tensor_copy(first_row[:, :], SMALL_PS[:, 32:32 + E]))
                nc.vector.tensor_scalar(reached[:, :], iota_j[0:E, :], first_col[:, 0:1], None, ALU.is_ge)\
                    .then_inc(first_copied, 1)
                dve.wait_ge(rank_done, 1)
                link(nc.vector.scalar_tensor_tensor(
                    slot, first_row[:, :].rearrange("p (o e) -> p o e", o=1).to_broadcast([P, NT, E]), float(P),
                    RANK_PS.rearrange("p (i e) -> p i e", e=E), ALU.mult, ALU.add))

            def slots_of_choices():
                for k in range(TOPK):
                    link(nc.vector.tensor_tensor(picked[:, :, :], chosen[:, k, :, :], slot, ALU.mult))
                    link(nc.vector.tensor_reduce(slot_k[:, k, :], picked[:, :, :], AX, ALU.add))
                link(nc.vector.tensor_copy(slot_i[:, :, :], slot_k[:, :, :]))
                nc.vector.tensor_scalar(slot_part_i[:, 0, :, :], slot_i[:, :, :], P - 1, None, ALU.bitwise_and)
                link(nc.vector.tensor_scalar(slot_part_i[:, 1, :, :], slot_i[:, :, :], P.bit_length() - 1, None,
                                             ALU.logical_shift_right))
                nc.vector.tensor_copy(slot_part[:, :, :, :], slot_part_i[:, :, :, :]).then_inc(slot_part_set, 1)

            def tables():
                dve.wait_ge(expert_done, 1)
                nc.vector.memset(tile_expert[:, 0:1], -1.0)
                link(nc.vector.tensor_scalar(tile_expert[:, 1:1 + TILES], EXPERT_PS[:, 64:64 + TILES], -1.0, None,
                                             ALU.add))
                link(nc.vector.tensor_copy(tile_expert_i[:, :], tile_expert[0:1, 1:1 + TILES]))
                link(nc.vector.tensor_tensor(to_split[:, 0, :], tile_expert[0:1, 1:1 + TILES],
                                             tile_expert[0:1, 0:TILES], ALU.subtract))
                link(nc.vector.scalar_tensor_tensor(to_split[:, 1, :], tile_expert[0:1, 1:1 + TILES],
                                                    float(E - SPLIT_AHEAD), to_split[:, 0, :], ALU.is_lt, ALU.mult))
                link(nc.vector.scalar_tensor_tensor(to_split[:, 0, :], tile_expert[0:1, 1:1 + TILES],
                                                    float(SPLIT_AHEAD), to_split[:, 1, :], ALU.add, ALU.mult))
                nc.vector.tensor_copy(to_split_i[:, :], to_split[:, 0, :]).then_inc(tables_set, 1)

            def weights():
                dve.wait_ge(scored, 1)
                dve.wait_ge(mask_set, 1)
                link(nc.vector.tensor_tensor(score, mask[:, :, :], score, ALU.mult))
                link(nc.vector.tensor_reduce(wsum[:, :], score, AX, ALU.add))
                link(nc.vector.tensor_scalar(wsum[:, :], wsum[:, :], 1e-20, None, ALU.add))
                link(nc.vector.reciprocal(wrec[:, :], wsum[:, :]))
                nc.vector.tensor_tensor(combine, score, wrec[:, :].rearrange("p (i o) -> p i o", o=1)
                                        .to_broadcast([P, NT, E]), ALU.mult).then_inc(combine_set, 1)

            def one_hots(k, part):
                n = k * (NT // HOTS) + part
                dve.wait_ge(slot_part_set, 1)
                if n >= 2:
                    dve.wait_ge(found_done, n - 1)
                for h in range(HOTS):
                    i = part * HOTS + h
                    last = nc.vector.tensor_scalar(hots[:, n % 2, h, 1, :], iota_j[:, :], slot_part[:, 1, k, i:i + 1],
                                                   token_no[:, i:i + 1], ALU.is_equal, ALU.mult)
                last.then_inc(tile_hots_set, 1)

            between = {1: [count_tiles], 2: [first_tiles], 3: [slots_of_choices], 4: [tables, weights]}

            def add_x(i):
                g = i // GT
                if i % GT == 0:
                    dve.wait_ge(x_in[g % 2], 16 * (NG // 2 + g // 2 + 1))
                dve.wait_ge(sd_done, i + 1)
                if i >= 2:
                    dve.wait_ge(s_stored[i % 2], 16 * (i // 2))
                nc.vector.tensor_tensor(s_sum[:, i % 2, :], SD_PS[i % 2][:, :], x_sb[:, g % 2, i % GT, :],
                                        ALU.add).then_inc(s_sum_set, 1)

            for n in range(4):
                dve.wait_ge(y_stored[n], 16 * NT // 4)
            for n in range(STEPS):
                g, f = n // SC, n % SC
                dve.wait_ge(s_silu_set, n + 1)
                dve.wait_ge(su_done, n + 1)
                nc.vector.tensor_tensor(hid_f[:, n % 2, :], hid_f[:, n % 2, :], SU_PS[n % 2][:, :],
                                        ALU.mult).then_inc(hid_set, 1)
                k = n + 1 - HOT_STEP
                if 0 <= k < TOPK:
                    one_hots(k, 0)
                    one_hots(k, 1)
                if f == 0 and g >= 1:
                    for i in range(GT * (g - 1), GT * g):
                        add_x(i)
                dve.wait_ge(hid_hi_set, n + 1)
                subtract(hid[1][:, f, :], hid_f[:, n % 2, :], hid[0][:, f, :]).then_inc(hid_lo_set, 1)
                if 0 <= k < TOPK:
                    for part in range(2, NT // HOTS):
                        one_hots(k, part)
                for routing in between.get(n, []):
                    routing()
            dve.wait_ge(found_done, SETS)
            link(nc.vector.tensor_copy(found[:, :], SLOT_PS[:, 0:TILES]))
            link(nc.vector.scalar_tensor_tensor(spare[:, :], found[:, :], 0.0, spare[:, :], ALU.is_equal, ALU.mult))
            nc.vector.scalar_tensor_tensor(slot_token[:, :], found[:, :], -1.0, spare[:, :],
                                           ALU.add, ALU.add).then_inc(slots_set, 1)

            def gate_up_low(e):
                dve.wait_ge(gu_hi_set, e + 1)
                whole, hi, lo = gate_up_parts(e)
                subtract(lo, whole, hi).then_inc(gu_lo_set, 1)

            def down_low(e):
                dve.wait_ge(d_hi_set, e + 1)
                whole, hi, lo = down_parts(e)
                subtract(lo, whole, hi).then_inc(d_lo_set, 1)

            for i in range(NT - GT, NT - 2):
                add_x(i)
            gate_up_low(0)
            add_x(NT - 2)
            down_low(0)
            add_x(NT - 1)

            def weigh(q, s):
                j, q, s = tile(q, s)
                dve.wait_ge(row_in[s], (q + 1) * 16)
                if not first(j, 2):
                    dve.wait_ge(act_set, j - 1)
                if not first(j, 1):
                    dve.wait_ge(weight_set, j)
                nc.vector.scalar_tensor_tensor(
                    hot[:, :], iota_e[:, :], tile_expert[:, ds(j + 1, 1)], row[:, s, H:ROW],
                    ALU.is_equal, ALU.mult, accum_out=weight[:, s % 2:s % 2 + 1]).then_inc(weight_set, 1)

            def rowT_low(q, s):
                j, q, s = tile(q, s)
                dve.wait_ge(rowT_hi_set, j + 1)
                subtract(rowT[1][:, s % 2, :, :], XT_PS[s % 2].rearrange("p (c t) -> p c t", c=HC),
                         rowT[0][:, s % 2, :, :]).then_inc(rowT_lo_set, 1)

            split_at = {}

            def to_split_at(j):
                return dve.value_load(to_split_i[0:1, ds(j, 1)], min_val=0, max_val=E - 1)

            def actT_low(q, s):
                j, q, s = tile(q, s)
                dve.wait_ge(actT_hi_set, j + 1)
                subtract(actT[1][:, s % 2, :, :], AT_PS[s % 2][0:FP, 0:FC * P].rearrange("p (c t) -> p c t", c=FC),
                         actT[0][:, s % 2, :, :]).then_inc(actT_lo_set, 1)

            def step(q, s):
                j = q * UNROLL + s
                if first(j, 1):
                    for n in range(2):
                        rowT_low(0, n)
                        weigh(0, n)
                    gate_up_low(1)
                    down_low(1)
                dve.wait_ge(silu_set, j + 1)
                dve.wait_ge(weight_set, j + 1)
                nc.vector.scalar_tensor_tensor(
                    act_sb[:, s % 2, :], act_sb[:, s % 2, :], weight[:, s % 2:s % 2 + 1], GU_PS[s % 2][:, F:2 * F],
                    ALU.mult, ALU.mult).then_inc(act_set, 1)
                if not first(j, 1):
                    actT_low(q, s - 1)
                if exists(j + 2):
                    rowT_low(q, s + 2)
                    weigh(q, s + 2)
                if not first(j, 1):
                    e = split_at[s - 1] if s else to_split_at(j - 1)
                    with dve.If(e > 0):
                        down_low(e)
                e = to_split_at(j)
                with dve.If(e > 0):
                    gate_up_low(e)
                if s < UNROLL - 1:
                    split_at[s] = e

            over_tiles(dve, step)
            actT_low(LAST, UNROLL - 1)

            for g in range(NG):
                dve.wait_ge(sums_in[g % 2], 32 * (g // 2 + 1))
                second = raw_ring[:, g % 2, 0:GT * H].rearrange("p (i h) -> p i h", h=H)
                nc.vector.tensor_tensor(x_sb[:, g % 2, :, :], x_sb[:, g % 2, :, :], second, ALU.add)\
                    .then_inc(total_set, 1)

        @block.tensor
        def _(pe):
            def three_passes(out_ps, operands):
                terms = [(st[a], mv[b]) for st, mv in operands for a, b in ((0, 0), (0, 1), (1, 0))]
                for n, (st, mv) in enumerate(terms):
                    last = nc.tensor.matmul(out_ps, st, mv, start=(n == 0), stop=(n == len(terms) - 1))
                return last

            def y_transposes(i):
                pe.wait_ge(y_copied, i + 1)
                if i >= 2:
                    pe.wait_ge(yT_whole_set, i - 1)
                for c in range(HC):
                    last = nc.tensor.transpose(YT_PS[i % 2][:, c * P:(c + 1) * P], y_sb[:, i % 4, c * P:(c + 1) * P],
                                               ident[:, :])
                last.then_inc(yT_done, 1)

            def logits(i):
                pe.wait_ge(yT_whole_set, i + 1)
                if i >= 2:
                    pe.wait_ge(logits_copied, i - 1)
                for c in range(HC):
                    last = nc.tensor.matmul(LOGIT_PS[i % 2][:, 0:E], yT_whole[:, i % 2, c, :], gate[:, c, :],
                                            start=(c == 0), stop=(c == HC - 1))
                last.then_inc(logits_done, 1)

            pe.wait_ge(consts, 1)
            pe.wait_ge(gate_in, 16)
            for i in range(NT):
                if i % GT == 0:
                    g = i // GT
                    pe.wait_ge(mix_in[g], 16 * 2 * GT)
                    pe.wait_ge(x_in[g % 2], 16 * (g // 2 + 1))
                if i >= 2:
                    pe.wait_ge(y_copied, i - 1)
                nc.tensor.matmul(Y_PS[i % 2][:, :], mix[:, i, :], x_sb[:, i // GT % 2, i % GT, :],
                                 start=True, stop=True).then_inc(y_done, 1)
                if i >= 1:
                    y_transposes(i - 1)
                if i >= 2:
                    logits(i - 2)
            y_transposes(NT - 1)
            logits(NT - 2)
            logits(NT - 1)

            def count_and_rank():
                pe.wait_ge(consts, 7)
                pe.wait_ge(mask_set, 1)
                for i in range(NT):
                    last = nc.tensor.matmul(SMALL_PS[0:E, 0:1], mask[:, i, :], ones[:, 0:1],
                                            start=(i == 0), stop=(i == NT - 1))
                last.then_inc(count_done, 1)
                nc.tensor.matmul(RANK_PS[:, :], before[:, :], mask[:, :, :].rearrange("p i e -> p (i e)"),
                                 start=True, stop=False)
                for i in range(NT - 1):
                    last = nc.tensor.matmul(RANK_PS[:, (i + 1) * E:NT * E], ones[:, :],
                                            mask[:, i:i + 1, :].to_broadcast([P, NT - 1 - i, E]),
                                            start=False, stop=(i == NT - 2))
                last.then_inc(rank_done, 1)

            def first_tiles():
                pe.wait_ge(tiles_set, 1)
                nc.tensor.matmul(SMALL_PS[0:E, 1:2], before[0:E, 0:E], tiles_b[:, 0:1], start=True, stop=True)
                nc.tensor.matmul(SMALL_PS[:, 32:32 + E], tiles_b[:, :], before[0:E, 0:E], start=True, stop=True)\
                    .then_inc(first_done, 1)

            def experts_of_tiles():
                pe.wait_ge(first_copied, 1)
                nc.tensor.matmul(EXPERT_PS[:, 64:64 + TILES], ones[0:E, :], reached[:, :], start=True, stop=True)\
                    .then_inc(expert_done, 1)

            def find_tokens(k, part):
                n = k * (NT // HOTS) + part
                pe.wait_ge(place_hots_set, n + 1)
                pe.wait_ge(tile_hots_set, n + 1)
                for h in range(HOTS):
                    last = nc.tensor.matmul(SLOT_PS[:, 0:TILES], hots[:, n % 2, h, 0, :], hots[:, n % 2, h, 1, :],
                                            start=(n == 0 and h == 0), stop=(n == SETS - 1 and h == HOTS - 1))
                last.then_inc(found_done, 1)

            def shared_product(n, ps, at, done):
                g, f = n // SC, n % SC
                three_passes(ps[n % 2][:, :], [
                    ([w[:, c, at + f * P:at + (f + 1) * P] for w in sgu],
                     [y[:, c, g * GT * P:(g + 1) * GT * P] for y in yT]) for c in range(HC)]).then_inc(done, 1)

            def shared_down(g):
                pe.wait_ge(hid_lo_set, SC * (g + 1))
                for i in range(GT * g, GT * g + GT):
                    if i >= 2:
                        pe.wait_ge(s_sum_set, i - 1)
                    t = i % GT
                    three_passes(SD_PS[i % 2][:, :], [
                        ([h[:, f, t * P:(t + 1) * P] for h in hid], [w[:, f, :] for w in sdw])
                        for f in range(SC)]).then_inc(sd_done, 1)

            pe.wait_ge(shared_lo_set, len(SHARED_PIECES))
            between = {1: count_and_rank, 2: first_tiles, 3: experts_of_tiles}
            for n in range(STEPS):
                k = n - HOT_STEP
                if n % SC == 0:
                    pe.wait_ge(yT_lo_set, GT * (n // SC + 1))
                if n >= 2:
                    pe.wait_ge(hid_set, n - 1)
                shared_product(n, SG_PS, 0, sg_done)
                if k >= 0:
                    find_tokens(k, 0)
                    find_tokens(k, 1)
                shared_product(n, SU_PS, FS, su_done)
                if k >= 0:
                    find_tokens(k, 2)
                    find_tokens(k, 3)
                if n % SC == 0 and n > 0:
                    shared_down(n // SC - 1)
                if n in between:
                    between[n]()
            shared_down(NG - 1)

            pe.wait_ge(s_sum_set, NT)
            pe.wait_ge(tables_set, 1)
            pe.wait_ge(slots_set, 1)

            def expert_of(j):
                return pe.value_load(tile_expert_i[0:1, ds(j, 1)], min_val=0, max_val=E - 1)

            def row_transposes(q, s):
                j, q, s = tile(q, s)
                pe.wait_ge(row_in[s], (q + 1) * 16)
                if not first(j, 2):
                    pe.wait_ge(rowT_lo_set, j - 1)
                for c in range(HC):
                    last = nc.tensor.transpose(XT_PS[s % 2][:, c * P:(c + 1) * P], row[:, s, c * P:(c + 1) * P],
                                               ident[:, :])
                last.then_inc(rowT_done, 1)

            def gate_and_up(q, s, e):
                j, q, s = tile(q, s)
                pe.wait_ge(gu_lo_set, e + 1)
                pe.wait_ge(rowT_lo_set, j + 1)
                if not first(j, 2):
                    pe.wait_ge(act_set, j - 1)
                three_passes(GU_PS[s % 2][:, 0:2 * F], [
                    ([r[:, s % 2, c, :] for r in rowT],
                     [ring[:, ds(e % RING, 1), part, c * 2 * F:(c + 1) * 2 * F].rearrange("p r f -> p (r f)")
                      for part in range(2)]) for c in range(HC)]).then_inc(gu_done, 1)

            def down(q, s, e):
                j, q, s = tile(q, s)
                pe.wait_ge(d_lo_set, e + 1)
                pe.wait_ge(actT_lo_set, j + 1)
                if not first(j, 2):
                    pe.wait_ge(result_set, j - 1)
                three_passes(D_PS[s % 2][:, :], [
                    ([a[:, s % 2, c, :] for a in actT],
                     [ring[0:FP, ds(e % RING, 1), part, WGU + c * H:WGU + (c + 1) * H].rearrange("p r h -> p (r h)")
                      for part in range(2)]) for c in range(FC)]).then_inc(down_done, 1)

            def act_transposes(q, s):
                j, q, s = tile(q, s)
                pe.wait_ge(act_set, j + 1)
                if not first(j, 2):
                    pe.wait_ge(actT_lo_set, j - 1)
                for c in range(FC):
                    last = nc.tensor.transpose(AT_PS[s % 2][0:FP, c * P:(c + 1) * P],
                                               act_sb[:, s % 2, c * FP:(c + 1) * FP], ident[:, :])
                last.then_inc(actT_done, 1)

            experts = {}

            def step(q, s):
                j = q * UNROLL + s
                if first(j, 1):
                    row_transposes(0, 0)
                    row_transposes(0, 1)
                experts[s] = expert_of(j)
                gate_and_up(q, s, experts[s])
                if not first(j, 1):
                    act_transposes(q, s - 1)
                if exists(j + 2):
                    row_transposes(q, s + 2)
                if not first(j, 2):
                    down(q, s - 2, experts[s - 2] if s >= 2 else expert_of(j - 2))

            over_tiles(pe, step)
            act_transposes(LAST, UNROLL - 1)
            for s in range(UNROLL - 2, UNROLL):
                down(LAST, s, expert_of(LAST * UNROLL + s))


_INS = ['x', 'itok_B_1_198', 'L0_cond_weights', 'L0_ffn_gate_w', 'L0_ffn_wg', 'L0_ffn_wu', 'L0_ffn_wd',
        'L0_ffn_sg', 'L0_ffn_su', 'L0_ffn_sd']


def kernel(**inputs):
    import numpy as _np
    import concourse.bacc as _bacc
    from concourse import mybir as _mybir
    from concourse.bass_utils import run_bass_kernel_spmd as _run

    nc = _bacc.Bacc("TRN2", target_bir_lowering=False, num_devices=1)
    arrays, args = {}, []
    for name in _INS:
        a = _np.ascontiguousarray(inputs[name])
        arrays[f"in_{name}"] = a
        args.append(nc.dram_tensor(f"in_{name}", a.shape, _mybir.dt.from_np(a.dtype), kind="ExternalInput").ap())
    shape = inputs['x'].shape
    args.append(nc.dram_tensor("out_0", shape, _mybir.dt.float32, kind="ExternalOutput").ap())
    adaln_moe_kernel(nc, *args)
    r = _run(nc, [arrays], core_ids=[0])
    return r.results[0]["out_0"]
```
